# Optimizing a Trainium2 kernel written in Bass

```python
import numpy as np
import jax
import jax.numpy as jnp

def _softmax(x, axis=-1):
    return jax.nn.softmax(x, axis=axis)

def _gelu(x):
    return jax.nn.gelu(x, approximate=True)

def _silu(x):
    return jax.nn.silu(x)

def _sigmoid(x):
    return jax.nn.sigmoid(x)

def _layernorm(x, axis=-1, eps=1e-05):
    m = jnp.mean(x, axis=axis, keepdims=True)
    v = jnp.var(x, axis=axis, keepdims=True)
    return (x - m) / jnp.sqrt(v + eps)

def _scatter_add(tgt, idx, src, axis=0):
    return tgt.at[idx].add(src)

def _segment_sum(src, seg, n):
    return jax.ops.segment_sum(src, seg, n)
kernel_name = 'mk_cond_resid_d1_seqx_r4_3d6235'

def setup_inputs(seed: int=0):
    np.random.seed(seed)
    _w = jnp.asarray

    def _rec_inputs():
        import jax
        import jax.numpy as jnp
        _rk = jax.random.key(seed)
        x = -0.000125 + 0.9999 * jax.random.normal(jax.random.fold_in(_rk, 1), (64, 64, 1024), jnp.float32)
        _lenS = 64 - jax.random.randint(jax.random.fold_in(_rk, 7), (64,), 0, max(1, 64 // 4) + 1, jnp.int32)
        _lenS2 = 64 - jax.random.randint(jax.random.fold_in(_rk, 8), (64,), 0, max(1, 64 // 4) + 1, jnp.int32)
        itok_B_3_7 = jax.random.randint(jax.random.fold_in(_rk, 11), (64,), 3, 8, jnp.int32)
        return (x, itok_B_3_7)
    x, itok_B_3_7 = _rec_inputs()

    def _L0_cond_setup():
        import jax, jax.numpy as jnp
        import numpy as np
        RANK = 16
        ALPHA = 16.0
        SCALING = ALPHA / RANK
        N_ADAPTERS = 8
        IN_F = 1024
        OUT_F = 1024
        BATCH = 4
        SEQ = 512
        key = jax.random.key(seed)
        kx, ka, kb, ki = jax.random.split(key, 4)
        x = jax.random.normal(kx, (BATCH, SEQ, IN_F), dtype=jnp.float32)
        A = jax.random.normal(ka, (N_ADAPTERS, OUT_F, RANK), dtype=jnp.float32) * 0.02
        B = jax.random.normal(kb, (N_ADAPTERS, RANK, IN_F), dtype=jnp.float32) * 0.02
        adapter_ids = jax.random.randint(ki, (BATCH,), 0, N_ADAPTERS, dtype=jnp.int32)
        return {'x': x, 'A': A, 'B': B, 'adapter_ids': adapter_ids}
    _L0_cond_all = _L0_cond_setup()
    _L0_cond_in = {k: v for k, v in _L0_cond_all.items() if k in ('A', 'B')}
    del _L0_cond_all
    return {'x': x, 'itok_B_3_7': itok_B_3_7, 'L0_cond_A': _L0_cond_in['A'], 'L0_cond_B': _L0_cond_in['B']}

def reference(x, itok_B_3_7, L0_cond_A, L0_cond_B):
    import jax
    import jax.numpy as jnp

    def _L0_cond_ref(x, A, B, adapter_ids):
        import jax, jax.numpy as jnp
        import numpy as np
        RANK = 16
        ALPHA = 16.0
        SCALING = ALPHA / RANK
        N_ADAPTERS = 8
        IN_F = 1024
        OUT_F = 1024
        BATCH = 4
        SEQ = 512
        B_sel = B[adapter_ids]
        A_sel = A[adapter_ids]
        Bx = jnp.einsum('bni,bri->bnr', x, B_sel)
        out = jnp.einsum('bnr,bor->bno', Bx, A_sel)
        return out * SCALING
    x = x + _L0_cond_ref(x, L0_cond_A, L0_cond_B, itok_B_3_7)
    return x

_drawn_inputs = setup_inputs


def setup_inputs(seed=0):
    import zlib

    import numpy as np

    out = dict(_drawn_inputs(seed))
    spreads = {}
    factors = {}
    for name, (base, spread) in spreads.items():
        noise = np.random.default_rng([zlib.crc32(name.encode()), seed]).standard_normal(out[name].shape)
        drawn = base * np.exp(spread * noise) if base else spread * noise
        out[name] = jnp.asarray(drawn.astype(out[name].dtype))
    for name, factor in factors.items():
        out[name] = (out[name] * factor).astype(out[name].dtype)
    return out
```

```python
from contextlib import ExitStack

import numpy as np

import concourse.bass as bass
from concourse import mybir


def lora_kernel(nc: bass.Bass, x: bass.AP, ids: bass.AP, a_in: bass.AP, b_in: bass.AP, out: bass.AP):
    F32, F32R, I32 = mybir.dt.float32, mybir.dt.float32r, mybir.dt.int32
    ALU = mybir.AluOpType

    SEQS, SEQ, D = x.shape
    ADAPTERS, RANK, _ = b_in.shape
    P = 128
    CHUNKS = D // P
    PER_TILE = P // SEQ
    DUOS = SEQS // (2 * PER_TILE)
    DUO_SEQS = 2 * PER_TILE
    GROUP = 8
    GROUPS = DUOS // GROUP
    BANK = 512
    HALF = CHUNKS // 2
    Q = D // P
    QUAD = 2 * RANK
    K_UP = 4 * RANK
    A_PIECE = 2
    B_UNITS = 2
    A_UNITS = ADAPTERS

    UP_SHARE = (0, 2, 3, 3)

    rows = x.rearrange("s t d -> (s t) d")
    out_rows = out.rearrange("s t d -> (s t) d")

    ctx = ExitStack()
    with ctx:
        def sb(name, shape, dt=F32):
            return ctx.enter_context(nc.sbuf_tensor(name, shape, dt))

        def pb(name, shape):
            return ctx.enter_context(nc.psum_tensor(name, shape, F32))

        def sem(name):
            return ctx.enter_context(nc.semaphore(name))

        x_ring = sb("x_ring", [P, GROUP * 2 * D])
        a_nat = sb("a_nat", [P, ADAPTERS, Q, RANK])
        a_rep = sb("a_rep", [P, ADAPTERS, Q, K_UP])
        b_nat = sb("b_nat", [ADAPTERS * RANK, D])
        id_row = sb("id_row", [1, SEQS], I32)
        b_table = sb("b_table", [P, ADAPTERS * CHUNKS * RANK])
        a_high = [sb(f"a_high{i}", [K_UP, D], F32R) for i in range(2)]
        a_table = sb("a_table", [K_UP, ADAPTERS * D], F32R)
        rest_rows = sb("rest_rows", [K_UP, 1])
        ident = sb("ident", [P, P])
        x_t = [sb(f"x_t{i}", [P, CHUNKS, 2, P]) for i in range(2)]
        b_duo = [sb(f"b_duo{i}", [P, CHUNKS, 2, PER_TILE * QUAD]) for i in range(2)]
        bx_parts = [sb(f"bx_parts{i}", [K_UP, 2, PER_TILE, P], F32R) for i in range(2)]

        t_bank = [pb(f"t_bank{i}", [P, BANK]) for i in range(2)]
        bx_bank = [pb(f"bx_bank{i}", [P, BANK]) for i in range(2)]
        y_banks = [pb(f"y_banks{i}", [P, D]) for i in range(2)]

        ids_loaded = sem("ids_loaded")
        a_loaded = sem("a_loaded")
        b_loaded = sem("b_loaded")
        a_repeated = sem("a_repeated")
        x_loaded = [sem(f"x_loaded{i}") for i in range(GROUP)]
        stored = [sem(f"stored{i}") for i in range(GROUP)]
        ident_steps = sem("ident_steps")
        rest_steps = sem("rest_steps")
        parts_zeroed = sem("parts_zeroed")
        t_filled = sem("t_filled")
        t_copied = sem("t_copied")
        b_gathered = sem("b_gathered")
        bx_done = sem("bx_done")
        high_done = sem("high_done")
        parts_done = sem("parts_done")
        a_high_done = sem("a_high_done")
        y_filled = sem("y_filled")
        y_drained = sem("y_drained")

        block = ctx.enter_context(nc.Block())

        def x_slot(slot):
            return x_ring[:, slot * 2 * D:(slot + 1) * 2 * D].rearrange("p (t d) -> p t d", t=2)

        def duo_rows(dram, duo):
            return dram[duo * 2 * P:(duo + 1) * 2 * P, :].rearrange("(t p) d -> p t d", p=P)

        def read_ids(engine, duo):
            return nc.values_load_multi_w_load_instructions(id_row[0:1, bass.ds(duo * DUO_SEQS, DUO_SEQS)], engines=[engine.engine],
                                        min_val=0, max_val=ADAPTERS - 1)[1]

        @block.sync
        def _(sp):
            sp.dma_start(id_row[:, :], ids.rearrange("(o s) -> o s", o=1)).then_inc(ids_loaded, 16)
            sp.dma_start(b_nat[:, :], b_in.rearrange("a r i -> (a r) i")).then_inc(b_loaded, 16)
            sp.dma_start(x_slot(0), duo_rows(rows, 0)).then_inc(x_loaded[0], 16)
            sp.dma_start(a_nat[:, :, :, :].rearrange("p a q r -> p a (q r)"),
                         a_in.rearrange("a (p q) r -> p a (q r)", q=Q)).then_inc(a_loaded, 16)
            for duo in range(1, GROUP):
                sp.dma_start(x_slot(duo), duo_rows(rows, duo)).then_inc(x_loaded[duo], 16)
            for duo in range(DUOS):
                slot = duo % GROUP
                sp.wait_ge(y_drained, A_UNITS + 2 * (duo + 1))
                sp.dma_start(duo_rows(out_rows, duo), x_slot(slot)).then_inc(stored[slot], 16)
                nxt = duo - 1 + GROUP
                if duo >= 1 and nxt < DUOS:
                    sp.wait_ge(stored[nxt % GROUP], 16 * (nxt // GROUP))
                    sp.dma_start(x_slot(nxt % GROUP), duo_rows(rows, nxt)).then_inc(x_loaded[nxt % GROUP], 16)
            for slot in range(GROUP):
                sp.wait_ge(stored[slot], 16 * GROUPS)

        @block.gpsimd
        def _(pool):
            nc.gpsimd.memset(ident[:, :], 0.0).then_inc(ident_steps, 1)
            nc.gpsimd.memset(rest_rows[:, :], -1.0).then_inc(rest_steps, 1)
            pool.wait_ge(ident_steps, 1)
            nc.gpsimd.affine_select(out=ident[:, :], in_=ident[:, :], compare_op=ALU.not_equal, fill=1.0,
                                    base=0, pattern=[[-1, P]], channel_multiplier=1).then_inc(ident_steps, 1)
            for step, (first, fill) in enumerate([(3 * RANK, 0.0), (2 * RANK, -1.0), (RANK, 0.0)]):
                pool.wait_ge(rest_steps, step + 1)
                nc.gpsimd.affine_select(out=rest_rows[:, :], in_=rest_rows[:, :], compare_op=ALU.is_ge, fill=fill,
                                        base=-first, pattern=[[0, 1]], channel_multiplier=1).then_inc(rest_steps, 1)
            for i in range(2):
                nc.gpsimd.memset(bx_parts[i][:, :, :, :].bitcast(F32), 0.0).then_inc(parts_zeroed, 1)

        @block.tensor
        def _(pe):
            pe.wait_ge(ident_steps, 2)

            pe.wait_ge(b_loaded, 16)
            for unit in range(B_UNITS):
                for c in range(HALF):
                    last = nc.tensor.transpose(t_bank[unit][:, c * P:(c + 1) * P],
                                               b_nat[:, (unit * HALF + c) * P:(unit * HALF + c + 1) * P], ident[:, :])
                last.then_inc(t_filled, 1)

            for a in range(A_UNITS):
                pe.wait_ge(a_repeated, a // A_PIECE + 1)
                if a >= 2:
                    pe.wait_ge(y_drained, a - 1)
                for q in range(Q):
                    last = nc.tensor.transpose(y_banks[a % 2][0:K_UP, q * P:(q + 1) * P], a_rep[:, a, q, :], ident[:, :])
                last.then_inc(y_filled, 1)

            def transpose_unit(g, u, v):
                half, tile = v // 2, v % 2
                n = B_UNITS + 4 * (GROUP * g + u) + v
                if v == 0:
                    pe.wait_ge(x_loaded[u], 16 * (g + 1))
                pe.wait_ge(t_copied, n - 1)
                for c in range(HALF):
                    at = (u * 2 + tile) * D + (half * HALF + c) * P
                    last = nc.tensor.transpose(t_bank[v % 2][:, c * P:(c + 1) * P], x_ring[:, at:at + P], ident[:, :])
                last.then_inc(t_filled, 1)

            def down(g, u, chunks):
                duo = GROUP * g + u
                for c in chunks:
                    if c == 0:
                        pe.wait_ge(b_gathered, duo + 1)
                        if u >= 2:
                            pe.wait_ge(parts_done, duo - 1)
                    if c % HALF == 0:
                        pe.wait_ge(t_copied, B_UNITS + 4 * duo + 2 * (c // HALF + 1))
                    for tile in range(2):
                        last = nc.tensor.matmul(bx_bank[u % 2][64 * tile:64 * tile + PER_TILE * QUAD, 0:P],
                                                b_duo[u % 2][:, c, tile, :], x_t[u % 2][:, c, tile, :],
                                                start=(c == 0), stop=(c == CHUNKS - 1))
                if chunks[-1] == CHUNKS - 1:
                    last.then_inc(bx_done, 1)

            def up_steps(g, u):
                duo = GROUP * g + u
                adapters = read_ids(pe, duo)
                pe.wait_ge(parts_done, duo + 1)
                for tile in range(2):
                    pe.wait_ge(y_drained, A_UNITS + 2 * duo + tile - 1)
                    for s in range(PER_TILE):
                        for h in range(D // BANK):
                            last = nc.tensor.matmul(
                                y_banks[tile][:, h * BANK:(h + 1) * BANK], bx_parts[u % 2][:, tile, s, :],
                                a_table[:, bass.ds(adapters[tile * PER_TILE + s] * D + h * BANK, BANK)],
                                start=(s == 0), stop=(s == PER_TILE - 1))
                            if s == PER_TILE - 1 and h == D // BANK - 1:
                                last.then_inc(y_filled, 1)
                            yield

            def take(steps, n):
                for _ in range(n):
                    next(steps, None)

            with pe.Fori(0, GROUPS) as g:
                for v in range(4):
                    transpose_unit(g, 0, v)
                for u in range(GROUP):
                    up = up_steps(g, u - 1) if u else iter(())
                    for v in range(4):
                        if u + 1 < GROUP:
                            transpose_unit(g, u + 1, v)
                        take(up, UP_SHARE[v])
                        down(g, u, [2 * v, 2 * v + 1])
                for _ in up_steps(g, GROUP - 1):
                    pass

        @block.scalar
        def _(act):
            for unit in range(B_UNITS):
                act.wait_ge(t_filled, unit + 1)
                nc.scalar.copy(
                    b_table[:, :].rearrange("p (a c r) -> p c a r", a=ADAPTERS, c=CHUNKS)
                    [:, unit * HALF:(unit + 1) * HALF],
                    t_bank[unit][:, :].rearrange("p (c a r) -> p c a r", c=HALF, a=ADAPTERS)).then_inc(t_copied, 1)

            for a in range(A_UNITS):
                act.wait_ge(y_filled, a + 1)
                if a >= 2:
                    act.wait_ge(y_drained, a - 1)
                nc.scalar.copy(a_high[a % 2][:, :], y_banks[a % 2][0:K_UP, :]).then_inc(a_high_done, 1)

            act.wait_ge(ids_loaded, 16)
            act.wait_ge(t_copied, B_UNITS)
            act.wait_ge(parts_zeroed, 2)

            def gather(g, u):
                adapters = read_ids(act, GROUP * g + u)
                for k in range(DUO_SEQS):
                    tile, s = k // PER_TILE, k % PER_TILE
                    source = b_table[:, bass.ds(adapters[k] * (CHUNKS * RANK), CHUNKS * RANK)]
                    last = nc.scalar.copy(
                        b_duo[u % 2][:, :, tile, s * QUAD:(s + 1) * QUAD].rearrange("p c (e r) -> p c e r", e=2),
                        source.rearrange("p (c r) -> p c r", c=CHUNKS).unsqueeze(2)
                        .to_broadcast([P, CHUNKS, 2, RANK]))
                last.then_inc(b_gathered, 1)

            def copy_transposes(g, u):
                for v in range(4):
                    half, tile = v // 2, v % 2
                    act.wait_ge(t_filled, B_UNITS + 4 * (GROUP * g + u) + v + 1)
                    nc.scalar.copy(x_t[u % 2][:, half * HALF:(half + 1) * HALF, tile, :],
                                   t_bank[v % 2][:, :].rearrange("p (c n) -> p c n", c=HALF)).then_inc(t_copied, 1)

            def split_high(g, u):
                duo = GROUP * g + u
                act.wait_ge(bx_done, duo + 1)
                act.wait_ge(y_filled, A_UNITS + 2 * duo - 2)
                for k in range(DUO_SEQS):
                    tile, s = k // PER_TILE, k % PER_TILE
                    last = nc.scalar.copy(bx_parts[u % 2][0:QUAD, tile, s, s * SEQ:(s + 1) * SEQ],
                                          bx_bank[u % 2][64 * tile + QUAD * s:64 * tile + QUAD * (s + 1),
                                                         s * SEQ:(s + 1) * SEQ])
                last.then_inc(high_done, 1)

            with act.Fori(0, GROUPS) as g:
                gather(g, 0)
                copy_transposes(g, 0)
                for u in range(GROUP):
                    if u + 1 < GROUP:
                        gather(g, u + 1)
                        copy_transposes(g, u + 1)
                    split_high(g, u)

        @block.vector
        def _(dve):
            dve.wait_ge(a_loaded, 16)
            for a in range(0, ADAPTERS, A_PIECE):
                nc.vector.tensor_copy(
                    a_rep[:, a:a + A_PIECE, :, :].rearrange("p a q (e r) -> p (a q) e r", r=RANK),
                    a_nat[:, a:a + A_PIECE, :, :].rearrange("p a q r -> p (a q) r").unsqueeze(2)
                    .to_broadcast([P, A_PIECE * Q, K_UP // RANK, RANK])).then_inc(a_repeated, 1)
            dve.wait_ge(rest_steps, 4)
            for a in range(A_UNITS):
                dve.wait_ge(a_high_done, a + 1)
                nc.vector.scalar_tensor_tensor(
                    a_table[:, a * D:(a + 1) * D].rearrange("k (p q) -> k q p", q=Q),
                    a_high[a % 2][:, :].rearrange("k (q p) -> k q p", q=Q), rest_rows[:, 0:1],
                    y_banks[a % 2][0:K_UP, :].rearrange("k (q p) -> k q p", q=Q),
                    op0=ALU.mult, op1=ALU.add).then_inc(y_drained, 1)

            def split_rest(duo, parity):
                dve.wait_ge(high_done, duo + 1)
                for k in range(DUO_SEQS):
                    tile, s = k // PER_TILE, k % PER_TILE
                    cols = slice(s * SEQ, (s + 1) * SEQ)
                    last = nc.vector.tensor_tensor(
                        bx_parts[parity][QUAD:2 * QUAD, tile, s, cols],
                        bx_bank[parity][64 * tile + QUAD * s:64 * tile + QUAD * (s + 1), cols],
                        bx_parts[parity][0:QUAD, tile, s, cols], ALU.subtract)
                last.then_inc(parts_done, 1)

            def add_x(duo, slot):
                for tile in range(2):
                    dve.wait_ge(y_filled, A_UNITS + 2 * duo + tile + 1)
                    here = x_ring[:, bass.ds(slot * (2 * D) + tile * D, D)]
                    nc.vector.tensor_tensor(here, y_banks[tile][:, :], here, ALU.add).then_inc(y_drained, 1)

            with dve.Fori(0, GROUPS) as g:
                with dve.Fori(0, GROUP // 2) as two:
                    for parity in range(2):
                        slot = two * 2 + parity
                        split_rest(g * GROUP + slot, parity)
                        add_x(g * GROUP + slot, slot)


def kernel(x, itok_B_3_7, L0_cond_A, L0_cond_B):
    import concourse.bacc as bacc
    from concourse.bass_utils import run_bass_kernel_spmd

    nc = bacc.Bacc("TRN2", target_bir_lowering=False, num_devices=1)
    arrays, args = {}, []
    for name, a in (("x", x), ("ids", itok_B_3_7), ("A", L0_cond_A), ("B", L0_cond_B)):
        a = np.ascontiguousarray(a)
        arrays[f"in_{name}"] = a
        args.append(nc.dram_tensor(f"in_{name}", a.shape, mybir.dt.from_np(a.dtype), kind="ExternalInput").ap())
    out = nc.dram_tensor("out_y", x.shape, mybir.dt.float32, kind="ExternalOutput").ap()
    lora_kernel(nc, *args, out)
    return run_bass_kernel_spmd(nc, [arrays], core_ids=[0]).results[0]["out_y"]
```

```python
from contextlib import ExitStack

import numpy as np

import concourse.bass as bass
from concourse import mybir


def lora_kernel(nc: bass.Bass, x: bass.AP, ids: bass.AP, a_in: bass.AP, b_in: bass.AP, out: bass.AP):
    F32, F32R, I32 = mybir.dt.float32, mybir.dt.float32r, mybir.dt.int32
    ALU = mybir.AluOpType

    SEQS, SEQ, D = x.shape
    ADAPTERS, RANK, _ = b_in.shape
    P = 128
    CHUNKS = D // P
    PER_TILE = P // SEQ
    DUOS = SEQS // (2 * PER_TILE)
    DUO_SEQS = 2 * PER_TILE
    GROUP = 8
    GROUPS = DUOS // GROUP
    BANK = 512
    HALF = CHUNKS // 2
    Q = D // P
    ID_BITS = ADAPTERS.bit_length() - 1
    WORD_IDS = 2 * DUO_SEQS
    QUAD = 2 * RANK
    K_UP = 4 * RANK
    A_RING = 4
    BY_DVE = 3
    A_SPLITS = 3
    B_UNITS = 2
    A_UNITS = ADAPTERS
    A_BANKS = 4
    A_BY_ACT = [a for a in range(A_UNITS) if a % A_BANKS == 3]
    A_BY_DVE = [a for a in range(A_UNITS) if a % A_BANKS != 3]

    UP_SHARE = (0, 0, 2, 2)

    rows = x.rearrange("s t d -> (s t) d")
    out_rows = out.rearrange("s t d -> (s t) d")

    ctx = ExitStack()
    with ctx:
        def sb(name, shape, dt=F32):
            return ctx.enter_context(nc.sbuf_tensor(name, shape, dt))

        def pb(name, shape):
            return ctx.enter_context(nc.psum_tensor(name, shape, F32))

        def sem(name):
            return ctx.enter_context(nc.semaphore(name))

        x_ring = sb("x_ring", [P, GROUP * 2 * D])
        a_nat = sb("a_nat", [P, ADAPTERS, Q, RANK])
        a_parts = sb("a_parts", [P, ADAPTERS * Q, 4, RANK], F32R)
        b_nat = sb("b_nat", [ADAPTERS * RANK, D])
        id_row = sb("id_row", [1, SEQS], I32)
        id_words = sb("id_words", [1, 1 + DUOS // 2 + 1], I32)
        b_table = sb("b_table", [P, ADAPTERS * CHUNKS * RANK])
        a_table = sb("a_table", [K_UP, ADAPTERS * D], F32R)
        ident = sb("ident", [P, P])
        x_t = [sb(f"x_t{i}", [P, CHUNKS, 2, P]) for i in range(2)]
        b_duo = [sb(f"b_duo{i}", [P, CHUNKS, 2, PER_TILE * QUAD]) for i in range(2)]
        bx_parts = [sb(f"bx_parts{i}", [PER_TILE * K_UP, 2, P], F32R) for i in range(2)]
        a_duo = [sb(f"a_duo{i}", [PER_TILE * K_UP, 2, D], F32R) for i in range(A_RING)]

        a_ranks = a_nat[:, :, :, :].rearrange("p a q r -> p (a q) r")

        t_bank = [pb(f"t_bank{i}", [P, BANK]) for i in range(2)]
        bx_bank = [pb(f"bx_bank{i}", [P, BANK]) for i in range(2)]
        y_banks = [pb(f"y_banks{i}", [P, D]) for i in range(2)]

        ids_loaded = sem("ids_loaded")
        ids_packed = sem("ids_packed")
        a_loaded = sem("a_loaded")
        b_loaded = sem("b_loaded")
        a_rest_made = sem("a_rest_made")
        a_split = sem("a_split")
        x_loaded = [sem(f"x_loaded{i}") for i in range(GROUP)]
        stored = [sem(f"stored{i}") for i in range(GROUP)]
        last_stored = [sem(f"last_stored{i}") for i in range(2)]
        ident_steps = sem("ident_steps")
        parts_zeroed = sem("parts_zeroed")
        t_filled = sem("t_filled")
        t_copied = sem("t_copied")
        a_gathered_dve = sem("a_gathered_dve")
        a_gathered_act = sem("a_gathered_act")
        b_gathered = sem("b_gathered")
        bx_done = sem("bx_done")
        high_done = sem("high_done")
        parts_done = sem("parts_done")
        a_copied_act = sem("a_copied_act")
        y_filled = sem("y_filled")
        y_drained = sem("y_drained")

        block = ctx.enter_context(nc.Block())

        def x_slot(slot):
            return x_ring[:, slot * 2 * D:(slot + 1) * 2 * D].rearrange("p (t d) -> p t d", t=2)

        def duo_rows(dram, duo):
            return dram[duo * 2 * P:(duo + 1) * 2 * P, :].rearrange("(t p) d -> p t d", p=P)

        def read_word(engine, pair):
            return nc.values_load_multi_w_load_instructions(
                id_words[0:1, bass.ds(pair + 1, 1)], engines=[engine.engine],
                skip_runtime_bounds_check_because="unpack() masks what it takes from the word")[1][0]

        def unpack(word, parity):
            return [(word >> (ID_BITS * (parity * DUO_SEQS + k))) & (ADAPTERS - 1) for k in range(DUO_SEQS)]

        def a_bank(a):
            half = a % A_BANKS // 2
            return y_banks[a % 2][:, half * BANK:(half + 1) * BANK]

        def copy_a(copy, a):
            for odd in range(2):
                last = copy(a_table[:, a * D:(a + 1) * D].rearrange("k (p q e) -> k q p e", e=2, q=Q // 2)[:, :, :, odd],
                            a_bank(a)[odd * K_UP:(odd + 1) * K_UP, :].rearrange("k (q p) -> k q p", q=Q // 2))
            return last

        def gather_a(copy, adapters, k, buffer):
            tile, s = k // PER_TILE, k % PER_TILE
            return copy(a_duo[buffer][s * K_UP:(s + 1) * K_UP, tile, :], a_table[:, bass.ds(adapters[k] * D, D)])

        @block.sync
        def _(sp):
            sp.dma_start(id_row[:, :], ids.rearrange("(o s) -> o s", o=1)).then_inc(ids_loaded, 16)
            sp.dma_start(a_nat[:, :, :, :].rearrange("p a q r -> p a (q r)"),
                         a_in.rearrange("a (p q) r -> p a (q r)", q=Q)).then_inc(a_loaded, 16)
            sp.dma_start(b_nat[:, :], b_in.rearrange("a r i -> (a r) i")).then_inc(b_loaded, 16)
            for duo in range(GROUP):
                sp.dma_start(x_slot(duo), duo_rows(rows, duo)).then_inc(x_loaded[duo], 16)
            for duo in range(DUOS - 1):
                slot = duo % GROUP
                sp.wait_ge(y_drained, len(A_BY_DVE) + 2 * (duo + 1))
                sp.dma_start(duo_rows(out_rows, duo), x_slot(slot)).then_inc(stored[slot], 16)
                nxt = duo - 1 + GROUP
                if duo >= 1 and nxt < DUOS:
                    sp.wait_ge(stored[nxt % GROUP], 16 * (nxt // GROUP))
                    sp.dma_start(x_slot(nxt % GROUP), duo_rows(rows, nxt)).then_inc(x_loaded[nxt % GROUP], 16)
            for tile in range(2):
                sp.wait_ge(y_drained, len(A_BY_DVE) + 2 * (DUOS - 1) + tile + 1)
                sp.dma_start(duo_rows(out_rows, DUOS - 1)[:, tile, :],
                             x_slot(GROUP - 1)[:, tile, :]).then_inc(last_stored[tile], 16)
            for slot in range(GROUP - 1):
                sp.wait_ge(stored[slot], 16 * GROUPS)
            for tile in range(2):
                sp.wait_ge(last_stored[tile], 16)

        @block.gpsimd
        def _(pool):
            nc.gpsimd.memset(ident[:, :], 0.0).then_inc(ident_steps, 1)
            pool.wait_ge(ident_steps, 1)
            nc.gpsimd.affine_select(out=ident[:, :], in_=ident[:, :], compare_op=ALU.not_equal, fill=1.0,
                                    base=0, pattern=[[-1, P]], channel_multiplier=1).then_inc(ident_steps, 1)
            for i in range(2):
                nc.gpsimd.memset(bx_parts[i][:, :, :].bitcast(F32), 0.0).then_inc(parts_zeroed, 1)

        @block.tensor
        def _(pe):
            pe.wait_ge(ident_steps, 2)

            pe.wait_ge(b_loaded, 16)
            for unit in range(B_UNITS):
                for c in range(HALF):
                    last = nc.tensor.transpose(t_bank[unit][:, c * P:(c + 1) * P],
                                               b_nat[:, (unit * HALF + c) * P:(unit * HALF + c + 1) * P], ident[:, :])
                last.then_inc(t_filled, 1)

            def a_unit(a):
                if a == 0:
                    pe.wait_ge(a_split, A_SPLITS)
                before = a - A_BANKS
                if before in A_BY_ACT:
                    pe.wait_ge(a_copied_act, A_BY_ACT.index(before) + 1)
                if before in A_BY_DVE:
                    pe.wait_ge(y_drained, A_BY_DVE.index(before) + 1)
                for q in range(0, Q, 2):
                    last = nc.tensor.transpose(
                        a_bank(a)[:, q // 2 * P:(q // 2 + 1) * P],
                        a_parts[:, a * Q + q:a * Q + q + 2, :, :].rearrange("p q e r -> p (q e r)").bitcast(F32),
                        ident[:, :])
                last.then_inc(y_filled, 1)

            def transpose_unit(g, u, v):
                half, tile = v // 2, v % 2
                n = B_UNITS + 4 * (GROUP * g + u) + v
                if v == 0:
                    pe.wait_ge(x_loaded[u], 16 * (g + 1))
                pe.wait_ge(t_copied, n - 1)
                for c in range(HALF):
                    at = (u * 2 + tile) * D + (half * HALF + c) * P
                    last = nc.tensor.transpose(t_bank[v % 2][:, c * P:(c + 1) * P], x_ring[:, at:at + P], ident[:, :])
                last.then_inc(t_filled, 1)

            def down(g, u, chunks):
                duo = GROUP * g + u
                for c in chunks:
                    if c == 0:
                        pe.wait_ge(b_gathered, duo + 1)
                    if c % HALF == 0:
                        pe.wait_ge(t_copied, B_UNITS + 4 * duo + 2 * (c // HALF + 1))
                    for tile in range(2):
                        last = nc.tensor.matmul(bx_bank[u % 2][64 * tile:64 * tile + PER_TILE * QUAD, 0:P],
                                                b_duo[u % 2][:, c, tile, :], x_t[u % 2][:, c, tile, :],
                                                start=(c == 0), stop=(c == CHUNKS - 1))
                if chunks[-1] == CHUNKS - 1:
                    last.then_inc(bx_done, 1)

            def up_steps(duo, u):
                pe.wait_ge(parts_done, duo + 1)
                pe.wait_ge(a_gathered_dve, duo + 1)
                pe.wait_ge(a_gathered_act, duo + 1)
                for tile in range(2):
                    pe.wait_ge(y_drained, len(A_BY_DVE) + 2 * duo + tile - 1)
                    for h in range(D // BANK):
                        last = nc.tensor.matmul(y_banks[tile][:, h * BANK:(h + 1) * BANK], bx_parts[u % 2][:, tile, :],
                                                a_duo[u % A_RING][:, tile, h * BANK:(h + 1) * BANK],
                                                start=True, stop=True)
                        if h == D // BANK - 1:
                            last.then_inc(y_filled, 1)
                        yield

            def step(g, u, ahead=True, behind=True):
                up = up_steps(GROUP * g + u - 1, (u - 1) % GROUP) if behind else iter(())
                share = UP_SHARE if ahead else (0, 0, 0, 0)
                for v in range(4):
                    if ahead:
                        transpose_unit(g + (u + 1) // GROUP, (u + 1) % GROUP, v)
                    for a in A_SHARE[v] if not behind else ():
                        a_unit(a)
                    for _ in range(share[v]):
                        next(up, None)
                    down(g, u, [2 * v, 2 * v + 1])
                for _ in up:
                    pass

            transpose_unit(0, 0, 0)
            transpose_unit(0, 0, 1)
            a_unit(0)
            a_unit(1)
            transpose_unit(0, 0, 2)
            a_unit(2)
            transpose_unit(0, 0, 3)
            a_unit(3)
            A_SHARE = ((4, 5), (6, 7), (), ())

            with pe.Fori(0, GROUPS) as g:
                with pe.If(g):
                    step(g, 0)
                with pe.Else():
                    step(g, 0, behind=False)
                for u in range(1, GROUP - 1):
                    step(g, u)
                with pe.If(GROUPS - 1 - g):
                    step(g, GROUP - 1)
                with pe.Else():
                    step(g, GROUP - 1, ahead=False)
            for _ in up_steps(DUOS - 1, GROUP - 1):
                pass

        @block.scalar
        def _(act):
            act.wait_ge(a_loaded, 16)
            nc.scalar.copy(a_parts[:, :, 2, :], a_ranks).then_inc(a_split, 1)

            for unit in range(B_UNITS):
                act.wait_ge(t_filled, unit + 1)
                nc.scalar.copy(
                    b_table[:, :].rearrange("p (a c r) -> p c a r", a=ADAPTERS, c=CHUNKS)
                    [:, unit * HALF:(unit + 1) * HALF],
                    t_bank[unit][:, :].rearrange("p (c a r) -> p c a r", c=HALF, a=ADAPTERS)).then_inc(t_copied, 1)

            def copy_own(a):
                act.wait_ge(y_filled, a + 1)
                copy_a(nc.scalar.copy, a).then_inc(a_copied_act, 1)

            act.wait_ge(ids_packed, WORD_IDS - 1)
            act.wait_ge(t_copied, B_UNITS)
            act.wait_ge(parts_zeroed, 2)

            def gather_rest(adapters, buffer):
                for k in range(BY_DVE, DUO_SEQS):
                    last = gather_a(nc.scalar.copy, adapters, k, buffer)
                last.then_inc(a_gathered_act, 1)

            def prepare(g, u, adapters, a_after=None):
                for k in range(DUO_SEQS):
                    tile, s = k // PER_TILE, k % PER_TILE
                    source = b_table[:, bass.ds(adapters[k] * (CHUNKS * RANK), CHUNKS * RANK)]
                    last = nc.scalar.copy(
                        b_duo[u % 2][:, :, tile, s * QUAD:(s + 1) * QUAD].rearrange("p c (e r) -> p c e r", e=2),
                        source.rearrange("p (c r) -> p c r", c=CHUNKS).unsqueeze(2)
                        .to_broadcast([P, CHUNKS, 2, RANK]))
                    if k == DUO_SEQS - 1:
                        last.then_inc(b_gathered, 1)
                    half, tile = k // 2, k % 2
                    act.wait_ge(t_filled, B_UNITS + 4 * (GROUP * g + u) + k + 1)
                    nc.scalar.copy(x_t[u % 2][:, half * HALF:(half + 1) * HALF, tile, :],
                                   t_bank[k % 2][:, :].rearrange("p (c n) -> p c n", c=HALF)).then_inc(t_copied, 1)
                    if a_after and k in a_after:
                        copy_own(a_after[k])
                if a_after is None:
                    gather_rest(adapters, u % A_RING)

            def split_high(g, u):
                duo = GROUP * g + u
                act.wait_ge(bx_done, duo + 1)
                act.wait_ge(y_filled, A_UNITS + 2 * duo - 2)
                for k in range(DUO_SEQS):
                    tile, s = k // PER_TILE, k % PER_TILE
                    last = nc.scalar.copy(bx_parts[u % 2][s * K_UP:s * K_UP + QUAD, tile, s * SEQ:(s + 1) * SEQ],
                                          bx_bank[u % 2][64 * tile + QUAD * s:64 * tile + QUAD * (s + 1),
                                                         s * SEQ:(s + 1) * SEQ])
                last.then_inc(high_done, 1)

            first = unpack(read_word(act, 0), 0)
            prepare(0, 0, first, {3: 3})
            with act.Fori(0, GROUPS) as g:
                word = read_word(act, GROUP // 2 * g)
                with act.If(g):
                    prepare(g, 1, unpack(word, 1))
                    split_high(g, 0)
                with act.Else():
                    prepare(g, 1, unpack(word, 1), {1: 7})
                    act.wait_ge(y_drained, len(A_BY_DVE))
                    act.wait_ge(a_copied_act, len(A_BY_ACT))
                    gather_rest(unpack(read_word(act, 0), 0), 0)
                    split_high(g, 0)
                    gather_rest(unpack(read_word(act, 0), 1), 1)
                for u in range(1, GROUP - 1):
                    if u % 2:
                        word = read_word(act, GROUP // 2 * g + (u + 1) // 2)
                    prepare(g, u + 1, unpack(word, (u + 1) % 2))
                    split_high(g, u)
                with act.If(GROUPS - 1 - g):
                    prepare(g + 1, 0, unpack(read_word(act, GROUP // 2 * (g + 1)), 0))
                split_high(g, GROUP - 1)

        @block.vector
        def _(dve):
            dve.wait_ge(ids_loaded, 16)
            words = id_words[:, 1:1 + DUOS // 2]
            id_cols = id_row[:, :].rearrange("o (w i) -> o w i", i=WORD_IDS)
            for step, i in enumerate(reversed(range(WORD_IDS - 1))):
                if step:
                    dve.wait_ge(ids_packed, step)
                nc.vector.scalar_tensor_tensor(words, words if step else id_cols[:, :, WORD_IDS - 1], float(ADAPTERS),
                                               id_cols[:, :, i], op0=ALU.mult, op1=ALU.add).then_inc(ids_packed, 1)

            dve.wait_ge(a_loaded, 16)
            nc.vector.tensor_copy(a_parts[:, :, 0, :], a_ranks).then_inc(a_split, 1)
            dve.wait_ge(a_split, 2)
            nc.vector.tensor_tensor(a_parts[:, :, 1, :], a_ranks, a_parts[:, :, 0, :], ALU.subtract)\
                .then_inc(a_rest_made, 1)
            dve.wait_ge(a_rest_made, 1)
            nc.vector.tensor_copy(a_parts[:, :, 3, :], a_parts[:, :, 1, :]).then_inc(a_split, 1)
            for a in A_BY_DVE:
                dve.wait_ge(y_filled, a + 1)
                copy_a(nc.vector.tensor_copy, a).then_inc(y_drained, 1)

            def split_rest(duo, parity):
                dve.wait_ge(high_done, duo + 1)
                for k in range(DUO_SEQS):
                    tile, s = k // PER_TILE, k % PER_TILE
                    cols = slice(s * SEQ, (s + 1) * SEQ)
                    last = nc.vector.tensor_tensor(
                        bx_parts[parity][s * K_UP + QUAD:(s + 1) * K_UP, tile, cols],
                        bx_bank[parity][64 * tile + QUAD * s:64 * tile + QUAD * (s + 1), cols],
                        bx_parts[parity][s * K_UP:s * K_UP + QUAD, tile, cols], ALU.subtract)
                last.then_inc(parts_done, 1)

            def add_x(duo, slot):
                for tile in range(2):
                    dve.wait_ge(y_filled, A_UNITS + 2 * duo + tile + 1)
                    here = x_ring[:, bass.ds(slot * (2 * D) + tile * D, D)]
                    nc.vector.tensor_tensor(here, y_banks[tile][:, :], here, ALU.add).then_inc(y_drained, 1)

            def gather_share(adapters, buffer):
                for k in range(BY_DVE):
                    last = gather_a(nc.vector.tensor_copy, adapters, k, buffer)
                last.then_inc(a_gathered_dve, 1)

            dve.wait_ge(a_copied_act, len(A_BY_ACT))
            dve.wait_ge(y_drained, len(A_BY_DVE))
            gather_share(unpack(read_word(dve, 0), 0), 0)
            with dve.Fori(0, GROUPS) as g:
                with dve.Fori(0, GROUP // A_RING) as part:
                    for i in range(A_RING):
                        slot = part * A_RING + i
                        duo = g * GROUP + slot
                        pair = g * (GROUP // 2) + part * (A_RING // 2) + (i + 1) // 2
                        split_rest(duo, i % 2)
                        if i < A_RING - 1:
                            gather_share(unpack(read_word(dve, pair), (i + 1) % 2), i + 1)
                        else:
                            with dve.If(DUOS - 1 - duo):
                                gather_share(unpack(read_word(dve, pair), 0), 0)
                        add_x(duo, slot)


def kernel(x, itok_B_3_7, L0_cond_A, L0_cond_B):
    import concourse.bacc as bacc
    from concourse.bass_utils import run_bass_kernel_spmd

    nc = bacc.Bacc("TRN2", target_bir_lowering=False, num_devices=1)
    arrays, args = {}, []
    for name, a in (("x", x), ("ids", itok_B_3_7), ("A", L0_cond_A), ("B", L0_cond_B)):
        a = np.ascontiguousarray(a)
        arrays[f"in_{name}"] = a
        args.append(nc.dram_tensor(f"in_{name}", a.shape, mybir.dt.from_np(a.dtype), kind="ExternalInput").ap())
    out = nc.dram_tensor("out_y", x.shape, mybir.dt.float32, kind="ExternalOutput").ap()
    lora_kernel(nc, *args, out)
    return run_bass_kernel_spmd(nc, [arrays], core_ids=[0]).results[0]["out_y"]
```

```python
from contextlib import ExitStack

import numpy as np

import concourse.bass as bass
from concourse import mybir


def lora_kernel(nc: bass.Bass, x: bass.AP, ids: bass.AP, a_in: bass.AP, b_in: bass.AP, out: bass.AP):
    F32, F32R, I32 = mybir.dt.float32, mybir.dt.float32r, mybir.dt.int32
    ALU = mybir.AluOpType

    SEQS, SEQ, D = x.shape
    ADAPTERS, RANK, _ = b_in.shape
    P = 128
    CHUNKS = D // P
    PER_TILE = P // SEQ
    DUO_SEQS = 2 * PER_TILE
    DUOS = SEQS // DUO_SEQS
    TILES = 2 * DUOS
    GROUP = 8
    GROUPS = DUOS // GROUP
    SLOTS = 2 * GROUP
    LAG = 2
    BANK = 512
    HALF = CHUNKS // 2
    Q = D // P
    ID_BITS = ADAPTERS.bit_length() - 1
    WORD_IDS = 2 * DUO_SEQS
    QUAD = 2 * RANK
    K_UP = 4 * RANK
    B_UNITS = 2
    A_UNITS = ADAPTERS
    A_BANKS = 4
    A_SPLITS = 3
    A_BY_ACT = (1, 4)
    A_BY_DVE = [a for a in range(A_UNITS) if a not in A_BY_ACT]
    A_RING = 4
    BY_DVE = 3
    A_AFTER = 1

    UP_SHARE = (0, 0, 2, 2)
    LAST_UP_SHARE = (0, 0, 0, 2)
    A_SHARE = ((5,), (6,), (7,), ())

    rows = x.rearrange("s t d -> (s t) d")
    out_rows = out.rearrange("s t d -> (s t) d")

    ctx = ExitStack()
    with ctx:
        def sb(name, shape, dt=F32):
            return ctx.enter_context(nc.sbuf_tensor(name, shape, dt))

        def pb(name, shape):
            return ctx.enter_context(nc.psum_tensor(name, shape, F32))

        def sem(name):
            return ctx.enter_context(nc.semaphore(name))

        x_ring = sb("x_ring", [P, SLOTS * D])
        a_nat = sb("a_nat", [P, ADAPTERS, Q, RANK])
        a_parts = sb("a_parts", [P, ADAPTERS * Q, 4, RANK], F32R)
        b_nat = sb("b_nat", [ADAPTERS * RANK, D])
        id_row = sb("id_row", [1, SEQS], I32)
        id_words = sb("id_words", [1, 1 + DUOS // 2 + 1], I32)
        b_table = sb("b_table", [P, ADAPTERS * CHUNKS * RANK])
        a_table = sb("a_table", [K_UP, ADAPTERS * D], F32R)
        ident = sb("ident", [P, P])
        x_t = [sb(f"x_t{i}", [P, CHUNKS, 2, P]) for i in range(2)]
        b_duo = [sb(f"b_duo{i}", [P, CHUNKS, DUO_SEQS, QUAD]) for i in range(2)]
        bx_parts = [sb(f"bx_parts{i}", [PER_TILE * K_UP, 2, P], F32R) for i in range(2)]
        a_duo = [sb(f"a_duo{i}", [PER_TILE * K_UP, 2, D], F32R) for i in range(A_RING)]

        a_ranks = a_nat[:, :, :, :].rearrange("p a q r -> p (a q) r")

        t_bank = [pb(f"t_bank{i}", [P, BANK]) for i in range(2)]
        bx_bank = [pb(f"bx_bank{i}", [P, BANK]) for i in range(2)]
        y_banks = [pb(f"y_banks{i}", [P, D]) for i in range(2)]

        ids_loaded = sem("ids_loaded")
        ids_packed = sem("ids_packed")
        a_loaded = sem("a_loaded")
        b_loaded = sem("b_loaded")
        a_rest_made = sem("a_rest_made")
        a_split = sem("a_split")
        x_loaded = [sem(f"x_loaded{i}") for i in range(SLOTS)]
        stored = [sem(f"stored{i}") for i in range(SLOTS)]
        ident_steps = sem("ident_steps")
        parts_zeroed = sem("parts_zeroed")
        t_filled = sem("t_filled")
        t_copied = sem("t_copied")
        a_gathered_dve = sem("a_gathered_dve")
        a_gathered_rest = [sem(f"a_gathered_rest{i}") for i in range(A_RING)]
        b_gathered = sem("b_gathered")
        bx_done = sem("bx_done")
        high_done = sem("high_done")
        parts_done = sem("parts_done")
        a_copied_act = sem("a_copied_act")
        y_filled = sem("y_filled")
        y_drained = sem("y_drained")

        block = ctx.enter_context(nc.Block())

        def x_slot(slot):
            return x_ring[:, slot * D:(slot + 1) * D]

        def tile_rows(dram, tile):
            return dram[tile * P:(tile + 1) * P, :]

        def read_word(engine, pair):
            return nc.values_load_multi_w_load_instructions(
                id_words[0:1, bass.ds(pair + 1, 1)], engines=[engine.engine],
                skip_runtime_bounds_check_because="unpack() masks what it takes from the word")[1][0]

        def unpack(word, parity):
            return [(word >> (ID_BITS * (parity * DUO_SEQS + k))) & (ADAPTERS - 1) for k in range(DUO_SEQS)]

        def a_bank(a):
            half = a % A_BANKS // 2
            return y_banks[a % 2][:, half * BANK:(half + 1) * BANK]

        def copy_a(copy, a):
            for odd in range(2):
                outputs = a_table[:, a * D:(a + 1) * D].rearrange("k (p q e) -> k q p e", e=2, q=Q // 2)
                last = copy(outputs[:, :, :, odd],
                            a_bank(a)[odd * K_UP:(odd + 1) * K_UP, :].rearrange("k (q p) -> k q p", q=Q // 2))
            return last

        def gather_a(copy, adapters, k, buffer):
            tile, s = k // PER_TILE, k % PER_TILE
            return copy(a_duo[buffer][s * K_UP:(s + 1) * K_UP, tile, :], a_table[:, bass.ds(adapters[k] * D, D)])

        @block.sync
        def _(sp):
            sp.dma_start(a_nat[:, :, :, :].rearrange("p a q r -> p a (q r)"),
                         a_in.rearrange("a (p q) r -> p a (q r)", q=Q)).then_inc(a_loaded, 16)
            sp.dma_start(b_nat[:, :], b_in.rearrange("a r i -> (a r) i")).then_inc(b_loaded, 16)
            for tile in range(SLOTS):
                sp.dma_start(x_slot(tile), tile_rows(rows, tile)).then_inc(x_loaded[tile], 16)
            for tile in range(TILES):
                slot = tile % SLOTS
                sp.wait_ge(y_drained, len(A_BY_DVE) + tile + 1)
                sp.dma_start(tile_rows(out_rows, tile), x_slot(slot)).then_inc(stored[slot], 16)
                nxt = tile - LAG + SLOTS
                if tile >= LAG and nxt < TILES:
                    sp.wait_ge(stored[nxt % SLOTS], 16 * (nxt // SLOTS))
                    sp.dma_start(x_slot(nxt % SLOTS), tile_rows(rows, nxt)).then_inc(x_loaded[nxt % SLOTS], 16)
            for slot in range(SLOTS):
                sp.wait_ge(stored[slot], 16 * (TILES // SLOTS))

        @block.gpsimd
        def _(pool):
            nc.gpsimd.memset(ident[:, :], 0.0).then_inc(ident_steps, 1)
            pool.wait_ge(ident_steps, 1)
            nc.gpsimd.affine_select(out=ident[:, :], in_=ident[:, :], compare_op=ALU.not_equal, fill=1.0,
                                    base=0, pattern=[[-1, P]], channel_multiplier=1).then_inc(ident_steps, 1)
            for i in range(2):
                nc.gpsimd.memset(bx_parts[i][:, :, :].bitcast(F32), 0.0).then_inc(parts_zeroed, 1)

            pool.wait_ge(ids_packed, WORD_IDS - 1)
            word = read_word(pool, 0)
            pool.wait_ge(a_copied_act, len(A_BY_ACT))
            pool.wait_ge(y_drained, len(A_BY_DVE))
            for k in range(BY_DVE, DUO_SEQS):
                last = gather_a(nc.gpsimd.tensor_copy, unpack(word, 1), k, 1)
            last.then_inc(a_gathered_rest[1], 1)

            pool.wait_ge(y_filled, A_UNITS + 2 * (DUOS - A_RING))
            adapters = unpack(read_word(pool, DUOS // 2 - 1), 1)
            for k in range(BY_DVE):
                last = gather_a(nc.gpsimd.tensor_copy, adapters, k, A_RING - 1)
            last.then_inc(a_gathered_rest[A_RING - 1], 1)

        @block.tensor
        def _(pe):
            pe.wait_ge(ident_steps, 2)

            pe.wait_ge(b_loaded, 16)
            for unit in range(B_UNITS):
                for c in range(HALF):
                    last = nc.tensor.transpose(t_bank[unit][:, c * P:(c + 1) * P],
                                               b_nat[:, (unit * HALF + c) * P:(unit * HALF + c + 1) * P], ident[:, :])
                last.then_inc(t_filled, 1)

            def a_unit(a):
                if a == 0:
                    pe.wait_ge(a_split, A_SPLITS)
                before = a - A_BANKS
                if before in A_BY_ACT:
                    pe.wait_ge(a_copied_act, A_BY_ACT.index(before) + 1)
                if before in A_BY_DVE:
                    pe.wait_ge(y_drained, A_BY_DVE.index(before) + 1)
                for q in range(0, Q, 2):
                    last = nc.tensor.transpose(
                        a_bank(a)[:, q // 2 * P:(q // 2 + 1) * P],
                        a_parts[:, a * Q + q:a * Q + q + 2, :, :].rearrange("p q e r -> p (q e r)").bitcast(F32),
                        ident[:, :])
                last.then_inc(y_filled, 1)

            def transpose_unit(g, u, v):
                half, tile = v // 2, v % 2
                n = B_UNITS + 4 * (GROUP * g + u) + v
                if half == 0:
                    pe.wait_ge(x_loaded[2 * u + tile], 16 * (g + 1))
                pe.wait_ge(t_copied, n - 1)
                for c in range(HALF):
                    at = (u * 2 + tile) * D + (half * HALF + c) * P
                    last = nc.tensor.transpose(t_bank[v % 2][:, c * P:(c + 1) * P], x_ring[:, at:at + P], ident[:, :])
                last.then_inc(t_filled, 1)

            def down(g, u, chunks):
                duo = GROUP * g + u
                for c in chunks:
                    if c == 0:
                        pe.wait_ge(b_gathered, duo + 1)
                    if c % HALF == 0:
                        pe.wait_ge(t_copied, B_UNITS + 4 * duo + 2 * (c // HALF + 1))
                    for k in range(DUO_SEQS):
                        tile, s = k // PER_TILE, k % PER_TILE
                        last = nc.tensor.matmul(bx_bank[u % 2][k * QUAD:(k + 1) * QUAD, 0:SEQ],
                                                b_duo[u % 2][:, c, k, :],
                                                x_t[u % 2][:, c, tile, s * SEQ:(s + 1) * SEQ],
                                                start=(c == 0), stop=(c == CHUNKS - 1))
                if chunks[-1] == CHUNKS - 1:
                    last.then_inc(bx_done, 1)

            def up_steps(duo, u, gathers, by_dve=True):
                pe.wait_ge(parts_done, duo + 1)
                if by_dve:
                    pe.wait_ge(a_gathered_dve, duo + 1)
                pe.wait_ge(a_gathered_rest[u % A_RING], gathers)
                for tile in range(2):
                    pe.wait_ge(y_drained, len(A_BY_DVE) + 2 * duo + tile - 1)
                    for h in range(D // BANK):
                        last = nc.tensor.matmul(y_banks[tile][:, h * BANK:(h + 1) * BANK], bx_parts[u % 2][:, tile, :],
                                                a_duo[u % A_RING][:, tile, h * BANK:(h + 1) * BANK],
                                                start=True, stop=True)
                        if h == D // BANK - 1:
                            last.then_inc(y_filled, 1)
                        yield

            def step(g, u, ahead=True, behind=True):
                gathers = GROUP // A_RING * g + (u - 1) // A_RING + 1
                up = up_steps(GROUP * g + u - 1, (u - 1) % GROUP, gathers) if behind else iter(())
                share = UP_SHARE if ahead else LAST_UP_SHARE
                for v in range(4):
                    if ahead:
                        transpose_unit(g + (u + 1) // GROUP, (u + 1) % GROUP, v)
                    for a in A_SHARE[v] if not behind else ():
                        a_unit(a)
                    for _ in range(share[v]):
                        next(up, None)
                    down(g, u, [2 * v, 2 * v + 1])
                for _ in up:
                    pass

            a_unit(0)
            a_unit(1)
            transpose_unit(0, 0, 0)
            transpose_unit(0, 0, 1)
            a_unit(2)
            a_unit(3)
            transpose_unit(0, 0, 2)
            a_unit(4)
            transpose_unit(0, 0, 3)

            with pe.Fori(0, GROUPS) as g:
                with pe.If(g):
                    step(g, 0)
                with pe.Else():
                    step(g, 0, behind=False)
                for u in range(1, GROUP - 1):
                    step(g, u)
                with pe.If(GROUPS - 1 - g):
                    step(g, GROUP - 1)
                with pe.Else():
                    step(g, GROUP - 1, ahead=False)
            for _ in up_steps(DUOS - 1, GROUP - 1, DUOS // A_RING + 1, by_dve=False):
                pass

        @block.scalar
        def _(act):
            act.dma_start(id_row[:, :], ids.rearrange("(o s) -> o s", o=1)).then_inc(ids_loaded, 16)

            act.wait_ge(a_loaded, 16)
            nc.scalar.copy(a_parts[:, :, 2, :], a_ranks).then_inc(a_split, 1)

            for unit in range(B_UNITS):
                act.wait_ge(t_filled, unit + 1)
                nc.scalar.copy(
                    b_table[:, :].rearrange("p (a c r) -> p c a r", a=ADAPTERS, c=CHUNKS)
                    [:, unit * HALF:(unit + 1) * HALF],
                    t_bank[unit][:, :].rearrange("p (c a r) -> p c a r", c=HALF, a=ADAPTERS)).then_inc(t_copied, 1)

            def copy_own(a):
                act.wait_ge(y_filled, a + 1)
                copy_a(nc.scalar.copy, a).then_inc(a_copied_act, 1)

            def gather_rest(adapters, buffer):
                for k in range(BY_DVE, DUO_SEQS):
                    last = gather_a(nc.scalar.copy, adapters, k, buffer)
                last.then_inc(a_gathered_rest[buffer], 1)

            def prepare(g, u, adapters, with_a=True):
                for k in range(DUO_SEQS):
                    source = b_table[:, bass.ds(adapters[k] * (CHUNKS * RANK), CHUNKS * RANK)]
                    last = nc.scalar.copy(
                        b_duo[u % 2][:, :, k, :].rearrange("p c (e r) -> p c e r", e=2),
                        source.rearrange("p (c r) -> p c r", c=CHUNKS).unsqueeze(2)
                        .to_broadcast([P, CHUNKS, 2, RANK]))
                    if k == DUO_SEQS - 1:
                        last.then_inc(b_gathered, 1)
                    half, tile = k // 2, k % 2
                    act.wait_ge(t_filled, B_UNITS + 4 * (GROUP * g + u) + k + 1)
                    nc.scalar.copy(x_t[u % 2][:, half * HALF:(half + 1) * HALF, tile, :],
                                   t_bank[k % 2][:, :].rearrange("p (c n) -> p c n", c=HALF)).then_inc(t_copied, 1)
                    if with_a and k == A_AFTER:
                        gather_rest(adapters, u % A_RING)

            def split_high(g, u):
                duo = GROUP * g + u
                act.wait_ge(bx_done, duo + 1)
                act.wait_ge(y_filled, A_UNITS + 2 * duo - 2)
                for k in range(DUO_SEQS):
                    tile, s = k // PER_TILE, k % PER_TILE
                    last = nc.scalar.copy(bx_parts[u % 2][s * K_UP:s * K_UP + QUAD, tile, s * SEQ:(s + 1) * SEQ],
                                          bx_bank[u % 2][k * QUAD:(k + 1) * QUAD, 0:SEQ])
                last.then_inc(high_done, 1)

            copy_own(A_BY_ACT[0])
            act.wait_ge(ids_packed, WORD_IDS - 1)
            act.wait_ge(t_copied, B_UNITS)
            act.wait_ge(parts_zeroed, 2)
            prepare(0, 0, unpack(read_word(act, 0), 0), with_a=False)
            copy_own(A_BY_ACT[1])
            with act.Fori(0, GROUPS) as g:
                word = read_word(act, GROUP // 2 * g)
                with act.If(g):
                    prepare(g, 1, unpack(word, 1))
                    split_high(g, 0)
                with act.Else():
                    prepare(g, 1, unpack(word, 1), with_a=False)
                    act.wait_ge(y_drained, len(A_BY_DVE))
                    act.wait_ge(a_copied_act, len(A_BY_ACT))
                    gather_rest(unpack(read_word(act, 0), 0), 0)
                    split_high(g, 0)
                for u in range(1, GROUP - 1):
                    if u % 2:
                        word = read_word(act, GROUP // 2 * g + (u + 1) // 2)
                    prepare(g, u + 1, unpack(word, (u + 1) % 2))
                    split_high(g, u)
                with act.If(GROUPS - 1 - g):
                    prepare(g + 1, 0, unpack(read_word(act, GROUP // 2 * (g + 1)), 0))
                split_high(g, GROUP - 1)

        @block.vector
        def _(dve):
            dve.wait_ge(ids_loaded, 16)
            words = id_words[:, 1:1 + DUOS // 2]
            id_cols = id_row[:, :].rearrange("o (w i) -> o w i", i=WORD_IDS)
            for step, i in enumerate(reversed(range(WORD_IDS - 1))):
                if step:
                    dve.wait_ge(ids_packed, step)
                nc.vector.scalar_tensor_tensor(words, words if step else id_cols[:, :, WORD_IDS - 1], float(ADAPTERS),
                                               id_cols[:, :, i], op0=ALU.mult, op1=ALU.add).then_inc(ids_packed, 1)

            dve.wait_ge(a_loaded, 16)
            nc.vector.tensor_copy(a_parts[:, :, 0, :], a_ranks).then_inc(a_split, 1)
            dve.wait_ge(a_split, 2)
            nc.vector.tensor_tensor(a_parts[:, :, 1, :], a_ranks, a_parts[:, :, 0, :], ALU.subtract)\
                .then_inc(a_rest_made, 1)
            dve.wait_ge(a_rest_made, 1)
            nc.vector.tensor_copy(a_parts[:, :, 3, :], a_parts[:, :, 1, :]).then_inc(a_split, 1)

            for a in A_BY_DVE:
                dve.wait_ge(y_filled, a + 1)
                copy_a(nc.vector.tensor_copy, a).then_inc(y_drained, 1)

            def split_rest(duo, parity):
                dve.wait_ge(high_done, duo + 1)
                for k in range(DUO_SEQS):
                    tile, s = k // PER_TILE, k % PER_TILE
                    cols = slice(s * SEQ, (s + 1) * SEQ)
                    last = nc.vector.tensor_tensor(
                        bx_parts[parity][s * K_UP + QUAD:(s + 1) * K_UP, tile, cols],
                        bx_bank[parity][k * QUAD:(k + 1) * QUAD, 0:SEQ],
                        bx_parts[parity][s * K_UP:s * K_UP + QUAD, tile, cols], ALU.subtract)
                last.then_inc(parts_done, 1)

            def add_x(duo, slot, tiles=(0, 1)):
                for tile in tiles:
                    dve.wait_ge(y_filled, A_UNITS + 2 * duo + tile + 1)
                    here = x_ring[:, bass.ds(slot * (2 * D) + tile * D, D)]
                    nc.vector.tensor_tensor(here, y_banks[tile][:, :], here, ALU.add).then_inc(y_drained, 1)

            def gather_share(adapters, buffer):
                for k in range(BY_DVE):
                    last = gather_a(nc.vector.tensor_copy, adapters, k, buffer)
                last.then_inc(a_gathered_dve, 1)

            first = unpack(read_word(dve, 0), 0)
            dve.wait_ge(a_copied_act, len(A_BY_ACT))
            dve.wait_ge(y_drained, len(A_BY_DVE))
            gather_share(first, 0)
            with dve.Fori(0, GROUPS) as g:
                with dve.Fori(0, GROUP // A_RING) as part:
                    for i in range(A_RING):
                        slot = part * A_RING + i
                        duo = g * GROUP + slot
                        pair = g * (GROUP // 2) + part * (A_RING // 2) + (i + 1) // 2
                        if i < A_RING - 2:
                            split_rest(duo, i % 2)
                            gather_share(unpack(read_word(dve, pair), (i + 1) % 2), i + 1)
                            add_x(duo, slot)
                        elif i == A_RING - 2:
                            split_rest(duo, i % 2)
                            with dve.If(DUOS - 2 - duo):
                                gather_share(unpack(read_word(dve, pair), (i + 1) % 2), i + 1)
                                add_x(duo, slot)
                            with dve.Else():
                                add_x(duo, slot, (0,))
                                split_rest(duo + 1, (i + 1) % 2)
                                add_x(duo, slot, (1,))
                                add_x(duo + 1, slot + 1)
                        else:
                            with dve.If(DUOS - 1 - duo):
                                split_rest(duo, i % 2)
                                gather_share(unpack(read_word(dve, pair), 0), 0)
                                add_x(duo, slot)


def kernel(x, itok_B_3_7, L0_cond_A, L0_cond_B):
    import concourse.bacc as bacc
    from concourse.bass_utils import run_bass_kernel_spmd

    nc = bacc.Bacc("TRN2", target_bir_lowering=False, num_devices=1)
    arrays, args = {}, []
    for name, a in (("x", x), ("ids", itok_B_3_7), ("A", L0_cond_A), ("B", L0_cond_B)):
        a = np.ascontiguousarray(a)
        arrays[f"in_{name}"] = a
        args.append(nc.dram_tensor(f"in_{name}", a.shape, mybir.dt.from_np(a.dtype), kind="ExternalInput").ap())
    out = nc.dram_tensor("out_y", x.shape, mybir.dt.float32, kind="ExternalOutput").ap()
    lora_kernel(nc, *args, out)
    return run_bass_kernel_spmd(nc, [arrays], core_ids=[0]).results[0]["out_y"]
```
